# Optimizing a Trainium2 kernel written in Bass

```python
import numpy as np
import jax
import jax.numpy as jnp

def _softmax(x, axis=-1):
    return jax.nn.softmax(x, axis=axis)

def _gelu(x):
    return jax.nn.gelu(x, approximate=True)

def _silu(x):
    return jax.nn.silu(x)

def _sigmoid(x):
    return jax.nn.sigmoid(x)

def _layernorm(x, axis=-1, eps=1e-05):
    m = jnp.mean(x, axis=axis, keepdims=True)
    v = jnp.var(x, axis=axis, keepdims=True)
    return (x - m) / jnp.sqrt(v + eps)

def _scatter_add(tgt, idx, src, axis=0):
    return tgt.at[idx].add(src)

def _segment_sum(src, seg, n):
    return jax.ops.segment_sum(src, seg, n)
kernel_name = 'mk_adj_resnorm_d2_adj_r2_dc0820'

def setup_inputs(seed: int=0):
    np.random.seed(seed)
    _w = jnp.asarray

    def _rec_inputs():
        import jax
        import jax.numpy as jnp
        _gk = jax.random.key(seed)
        x = -0.0005207 + 1.001 * jax.random.normal(jax.random.fold_in(_gk, 1), (4096, 128), jnp.float32)
        _a = jax.random.bernoulli(jax.random.fold_in(_gk, 2), 0.000976562, (4096, 4096))
        _a = jnp.logical_or(_a, jnp.eye(4096, dtype=bool))
        _af = _a.astype(jnp.float32)
        _af = _af * jax.random.uniform(jax.random.fold_in(_gk, 3), (4096, 4096), jnp.float32, 0.05, 6.10351e-05)
        adj = _af
        return (x, adj)
    x, adj = _rec_inputs()

    def _L0_gnn_setup():
        import jax, jax.numpy as jnp
        import numpy as np
        N = 8192
        D = 128
        UNITS = 128
        key = jax.random.key(seed)
        k1, k2, k3 = jax.random.split(key, 3)
        x = jax.random.normal(k1, (N, D), dtype=jnp.float32)
        adj_norm = jax.random.uniform(k2, (N, N), dtype=jnp.float32) / N
        kernel = jax.random.normal(k3, (D, UNITS), dtype=jnp.float32) * (1.0 / np.sqrt(D))
        bias = jnp.zeros((UNITS,), dtype=jnp.float32)
        return {'x': x, 'adj_norm': adj_norm, 'kernel': kernel, 'bias': bias}
    _L0_gnn_all = _L0_gnn_setup()
    _L0_gnn_in = {k: v for k, v in _L0_gnn_all.items() if k in ('kernel', 'bias')}
    del _L0_gnn_all

    def _L1_gnn_setup():
        import jax, jax.numpy as jnp
        import numpy as np
        NEG_SLOPE = 0.01
        N_U, N_V = (4096, 4096)
        U_F, V_F = (128, 128)
        HIDS = [128, 128]
        NUM_ROUNDS = 3

        def _glorot(key, fan_in, fan_out):
            lim = np.sqrt(6.0 / (fan_in + fan_out)).astype(np.float32)
            return jax.random.uniform(key, (fan_in, fan_out), jnp.float32, -lim, lim)

        def _mlp(x, W1, b1, W2, b2, W3, b3):
            a = jax.nn.leaky_relu
            x = a(x @ W1 + b1, NEG_SLOPE)
            x = a(x @ W2 + b2, NEG_SLOPE)
            return a(x @ W3 + b3, NEG_SLOPE)
        key = jax.random.key(seed)
        ks = jax.random.split(key, 12)
        inp = {'u_node_feats': jax.random.normal(ks[0], (N_U, U_F), jnp.float32), 'v_node_feats': jax.random.normal(ks[1], (N_V, V_F), jnp.float32), 'uv_adj_mat': jax.random.uniform(ks[2], (N_V, N_U), jnp.float32), 'vu_adj_mat': jax.random.uniform(ks[3], (N_U, N_V), jnp.float32)}
        dims_uv = [U_F] + HIDS + [V_F]
        dims_vu = [V_F] + HIDS + [U_F]
        k = 4
        for tag, dims in (('uv', dims_uv), ('vu', dims_vu)):
            for i in range(3):
                inp[f'{tag}_W{i + 1}'] = _glorot(ks[k], dims[i], dims[i + 1])
                k += 1
                inp[f'{tag}_b{i + 1}'] = jnp.zeros((dims[i + 1],), jnp.float32)
        return inp
    _L1_gnn_all = _L1_gnn_setup()
    _L1_gnn_in = {k: v for k, v in _L1_gnn_all.items() if k in ('v_node_feats', 'uv_W1', 'uv_b1', 'uv_W2', 'uv_b2', 'uv_W3', 'uv_b3', 'vu_W1', 'vu_b1', 'vu_W2', 'vu_b2', 'vu_W3', 'vu_b3')}
    del _L1_gnn_all
    return {'x': x, 'adj': adj, 'L0_gnn_kernel': _L0_gnn_in['kernel'], 'L0_gnn_bias': _L0_gnn_in['bias'], 'L1_gnn_v_node_feats': _L1_gnn_in['v_node_feats'], 'L1_gnn_uv_W1': _L1_gnn_in['uv_W1'], 'L1_gnn_uv_b1': _L1_gnn_in['uv_b1'], 'L1_gnn_uv_W2': _L1_gnn_in['uv_W2'], 'L1_gnn_uv_b2': _L1_gnn_in['uv_b2'], 'L1_gnn_uv_W3': _L1_gnn_in['uv_W3'], 'L1_gnn_uv_b3': _L1_gnn_in['uv_b3'], 'L1_gnn_vu_W1': _L1_gnn_in['vu_W1'], 'L1_gnn_vu_b1': _L1_gnn_in['vu_b1'], 'L1_gnn_vu_W2': _L1_gnn_in['vu_W2'], 'L1_gnn_vu_b2': _L1_gnn_in['vu_b2'], 'L1_gnn_vu_W3': _L1_gnn_in['vu_W3'], 'L1_gnn_vu_b3': _L1_gnn_in['vu_b3']}

def reference(x, adj, L0_gnn_kernel, L0_gnn_bias, L1_gnn_v_node_feats, L1_gnn_uv_W1, L1_gnn_uv_b1, L1_gnn_uv_W2, L1_gnn_uv_b2, L1_gnn_uv_W3, L1_gnn_uv_b3, L1_gnn_vu_W1, L1_gnn_vu_b1, L1_gnn_vu_W2, L1_gnn_vu_b2, L1_gnn_vu_W3, L1_gnn_vu_b3):
    import jax
    import jax.numpy as jnp

    def _L0_gnn_ref(x, adj_norm, kernel, bias):
        import jax, jax.numpy as jnp
        import numpy as np
        N = 8192
        D = 128
        UNITS = 128
        agg = adj_norm @ x
        out = agg @ kernel + bias
        return jax.nn.relu(out)

    def _L1_gnn_ref(u_node_feats, v_node_feats, uv_adj_mat, vu_adj_mat, uv_W1, uv_b1, uv_W2, uv_b2, uv_W3, uv_b3, vu_W1, vu_b1, vu_W2, vu_b2, vu_W3, vu_b3):
        import jax, jax.numpy as jnp
        import numpy as np
        NEG_SLOPE = 0.01
        N_U, N_V = (4096, 4096)
        U_F, V_F = (128, 128)
        HIDS = [128, 128]
        NUM_ROUNDS = 3

        def _glorot(key, fan_in, fan_out):
            lim = np.sqrt(6.0 / (fan_in + fan_out)).astype(np.float32)
            return jax.random.uniform(key, (fan_in, fan_out), jnp.float32, -lim, lim)

        def _mlp(x, W1, b1, W2, b2, W3, b3):
            a = jax.nn.leaky_relu
            x = a(x @ W1 + b1, NEG_SLOPE)
            x = a(x @ W2 + b2, NEG_SLOPE)
            return a(x @ W3 + b3, NEG_SLOPE)
        u, v = (u_node_feats, v_node_feats)
        for _ in range(NUM_ROUNDS):
            v = _mlp(uv_adj_mat @ u, uv_W1, uv_b1, uv_W2, uv_b2, uv_W3, uv_b3)
            u = _mlp(vu_adj_mat @ v, vu_W1, vu_b1, vu_W2, vu_b2, vu_W3, vu_b3)
        return v
    x = _layernorm(x + _L0_gnn_ref(x, adj, L0_gnn_kernel, L0_gnn_bias), axis=-1)
    x = _layernorm(x + _L1_gnn_ref(x, L1_gnn_v_node_feats, adj, adj, L1_gnn_uv_W1, L1_gnn_uv_b1, L1_gnn_uv_W2, L1_gnn_uv_b2, L1_gnn_uv_W3, L1_gnn_uv_b3, L1_gnn_vu_W1, L1_gnn_vu_b1, L1_gnn_vu_W2, L1_gnn_vu_b2, L1_gnn_vu_W3, L1_gnn_vu_b3), axis=-1)
    return x

_drawn_inputs = setup_inputs


def setup_inputs(seed=0):
    import zlib

    import numpy as np

    out = dict(_drawn_inputs(seed))
    spreads = {'L0_gnn_bias': (0.0, 0.1),
     'L1_gnn_uv_b1': (0.0, 0.302),
     'L1_gnn_uv_b2': (0.0, 0.1),
     'L1_gnn_uv_b3': (0.0, 0.1),
     'L1_gnn_vu_b1': (0.0, 0.8),
     'L1_gnn_vu_b2': (0.0, 0.8),
     'L1_gnn_vu_b3': (0.0, 0.8)}
    factors = {'L1_gnn_uv_W1': 4.434, 'L1_gnn_vu_W1': 8.0, 'L1_gnn_vu_W2': 8.0, 'L1_gnn_vu_W3': 8.0}
    for name, (base, spread) in spreads.items():
        noise = np.random.default_rng([zlib.crc32(name.encode()), seed]).standard_normal(out[name].shape)
        drawn = base * np.exp(spread * noise) if base else spread * noise
        out[name] = jnp.asarray(drawn.astype(out[name].dtype))
    for name, factor in factors.items():
        out[name] = (out[name] * factor).astype(out[name].dtype)
    return out
```

```python
import concourse.bass as bass
from concourse import mybir
from contextlib import ExitStack

F32 = mybir.dt.float32
F32R = mybir.dt.float32r
ALU = mybir.AluOpType
ACT = mybir.ActivationFunctionType

P = 128
CHUNK = 512
TILES = CHUNK // P
EPS = 1e-5
SLOPE = 0.01

PIECE = 2 * CHUNK
LOAD = 2 * PIECE
LOAD_SLOTS = 4
SPLIT_SLOTS = 4

PE_LAYER = (3, 6, 9)
PE_GCN = 3
ACT_AGG, ACT_HID, ACT_STD = 3, (6, 9), 11
DVE_AGG, DVE_HID, DVE_PRE, DVE_FEAT = 3, (6, 9), 12, 13
DVE_SUM = {"gcn": 6, "last": 13}
DVE_NORM = {"gcn": 11, "last": 15}
POOL_HID, POOL_FEAT = (7, 10), 13
POOL_PIECES = (2, 7, 12)


def gnn_kernel(nc, x, adj, gcn_w, gcn_b, uv, vu, out):
    C = x.shape[0]
    PIECES = C * TILES * CHUNK // PIECE
    LOADS = PIECES * PIECE // LOAD
    DVE_PIECES = tuple(i for i in range(PIECES) if i not in POOL_PIECES)
    assert LOADS == C == adj.shape[1] and LOADS % LOAD_SLOTS == 0 and PIECES % SPLIT_SLOTS == 0

    GCN, UV, VU, LAST = "gcn", "uv", "vu", "last"
    PASSES = 6
    weights = [gcn_w, uv["W1"], uv["W2"], uv["W3"], vu["W1"], vu["W2"], vu["W3"]]
    LAYERS = {GCN: (0,), UV: (1, 2, 3), VU: (4, 5, 6), LAST: (1, 2, 3)}
    bias_cols = [uv["b1"], uv["b2"], vu["b1"], vu["b2"]]
    HID_BIAS = {UV: (0, 1), VU: (2, 3), LAST: (0, 1)}
    bias_rows = [gcn_b, uv["b3"], vu["b3"]]
    PRE_BIAS = {GCN: 0, UV: 1, VU: 2, LAST: 1}
    N_W = len(weights)
    N_PARAMS = N_W + len(bias_cols) + len(bias_rows)

    ctx = ExitStack()
    with ctx:
        def sb(name, shape, dt=F32):
            return ctx.enter_context(nc.sbuf_tensor(name, shape, dt))

        def ps(name, shape):
            return ctx.enter_context(nc.psum_tensor(name, shape, F32))

        def sem(name):
            return ctx.enter_context(nc.semaphore(name))

        adj_raw = sb("adj_raw", [P, LOAD_SLOTS, LOAD])
        adj_kept = sb("adj_kept", [P, C * PIECE])
        adj_hi = sb("adj_hi", [P, SPLIT_SLOTS, PIECE], F32R)
        adj_lo = sb("adj_lo", [P, SPLIT_SLOTS, PIECE], F32R)
        feat_hi = [sb(f"feat_hi{b}", [P, C * CHUNK], F32R) for b in range(2)]
        feat_lo = [sb(f"feat_lo{b}", [P, C * CHUNK], F32R) for b in range(2)]
        resid = sb("resid", [P, C * CHUNK])
        w_raw = sb("w_raw", [P, N_W, P])
        w_hi = sb("w_hi", [P, N_W, P], F32R)
        w_lo = sb("w_lo", [P, N_W, P], F32R)
        b_col = sb("b_col", [P, len(bias_cols)])
        b_row = sb("b_row", [P, len(bias_rows), P])
        agg_hi = sb("agg_hi", [P, CHUNK], F32R)
        agg_lo = sb("agg_lo", [P, CHUNK], F32R)
        hid_pre = sb("hid_pre", [P, CHUNK])
        hid = sb("hid", [P, CHUNK])
        hid_hi = sb("hid_hi", [P, CHUNK], F32R)
        hid_lo = sb("hid_lo", [P, CHUNK], F32R)
        pre = sb("pre", [P, CHUNK])
        post = sb("post", [P, CHUNK])
        summed = sb("summed", [P, CHUNK])
        stats = sb("stats", [P, TILES, 6])
        mean_var = sb("mean_var", [P, TILES, 2])
        std = sb("std", [P, TILES])
        rstd = sb("rstd", [P, TILES])
        eps = sb("eps", [P, 1])

        agg_ps = ps("agg_ps", [P, 2 * CHUNK])
        hid_ps = [ps(f"hid_ps{n}", [P, CHUNK]) for n in range(2)]
        pre_ps = ps("pre_ps", [P, CHUNK])

        x_loaded = [sem(f"x_loaded{g}") for g in range(C)]
        adj_loaded = [sem(f"adj_loaded{s}") for s in range(LOAD_SLOTS)]
        kept_loaded = sem("kept_loaded")
        params_loaded = sem("params_loaded")
        eps_ready = sem("eps_ready")
        w_hi_ready = sem("w_hi_ready")
        w_lo_ready = sem("w_lo_ready")
        adj_hi_ready = sem("adj_hi_ready")
        adj_lo_by_dve = sem("adj_lo_by_dve")
        adj_lo_by_pool = sem("adj_lo_by_pool")
        piece_used = sem("piece_used")
        feat_hi_ready = sem("feat_hi_ready")
        feat_lo_ready = sem("feat_lo_ready")
        agg_hi_ready = sem("agg_hi_ready")
        agg_lo_ready = sem("agg_lo_ready")
        hid_done = [sem(f"hid_done{n}") for n in range(2)]
        hid_pre_ready = [sem(f"hid_pre_ready{n}") for n in range(2)]
        hid_ready = [sem(f"hid_ready{n}") for n in range(2)]
        hid_hi_ready = [sem(f"hid_hi_ready{n}") for n in range(2)]
        hid_lo_ready = [sem(f"hid_lo_ready{n}") for n in range(2)]
        pre_done = sem("pre_done")
        pre_ready = sem("pre_ready")
        post_ready = sem("post_ready")
        sum_ready = sem("sum_ready")
        stats_ready = sem("stats_ready")
        var_ready = sem("var_ready")
        std_ready = sem("std_ready")
        rstd_ready = sem("rstd_ready")
        normed = sem("normed")
        out_written = sem("out_written")

        def block_of(t, chunk):
            return t[:, bass.ds(chunk * CHUNK, CHUNK)]

        def by_tile(ap):
            return ap.rearrange("p (j f) -> p j f", f=P)

        def raw_piece(chunk, i):
            if i == PIECES - 1:
                return adj_kept[:, bass.ds(chunk * PIECE, PIECE)]
            return adj_raw[:, (i // 2) % LOAD_SLOTS, (i % 2) * PIECE:(i % 2 + 1) * PIECE]

        def agg_bank(chunk):
            return agg_ps[:, bass.ds((chunk % 2) * CHUNK, CHUNK)]

        def walk(eng, step):
            step(0, 0, 0, None, None, None)
            with eng.Fori(1, C) as c:
                step(c, c, 0, GCN, c - 1, 1)
            step(C, 0, 1, GCN, C - 1, 1)
            with eng.Fori(C, C * (PASSES - 1), 2 * C) as q0:
                with eng.Fori(1, C) as c:
                    step(q0 + c, c, 1, UV, c - 1, 0)
                step(q0 + C, 0, 0, UV, C - 1, 0)
                with eng.Fori(1, C) as c:
                    step(q0 + C + c, c, 0, VU, c - 1, 1)
                step(q0 + 2 * C, 0, 1, VU, C - 1, 1)
            with eng.Fori(1, C) as c:
                step(C * (PASSES - 1) + c, c, 1, LAST, c - 1, None)
            step(C * PASSES, None, None, LAST, C - 1, None)

        def is_first(q):
            return isinstance(q, int) and q == 0

        def in_first_pass(q, kind):
            return is_first(q) or (kind == GCN and not isinstance(q, int))

        def mlps(q):
            return q - C

        def blocks(q):
            return q + C

        def norms(q, kind):
            return q if kind == GCN else q - C * (PASSES - 2)

        def lo_counts(pieces, last):
            return sum(i <= last for i in pieces)

        block = ctx.enter_context(nc.Block())

        @block.sync
        def _(sp):
            def wait_split(q, last):
                by_dve = q * len(DVE_PIECES) + lo_counts(DVE_PIECES, last)
                by_pool = q * len(POOL_PIECES) + lo_counts(POOL_PIECES, last)
                if not isinstance(q, int):
                    by_dve, by_pool = sp.snap(sp.to_reg(by_dve)), sp.snap(sp.to_reg(by_pool))
                sp.wait_ge(adj_lo_by_dve, by_dve)
                if not is_first(q) or by_pool:
                    sp.wait_ge(adj_lo_by_pool, by_pool)

            def step(q, chunk, src, kind, ended, dst):
                if chunk is None:
                    return
                for g in range(LOADS):
                    if is_first(q):
                        sp.dma_start(block_of(resid, g), x[g]).then_inc(x_loaded[g], 16)
                    if g >= LOAD_SLOTS:
                        wait_split(q, 2 * (g - LOAD_SLOTS) + 1)
                    elif not is_first(q):
                        wait_split(q - 1, 2 * (g - LOAD_SLOTS + LOADS) + 1)
                    width = LOAD if g < LOADS - 1 else LOAD - PIECE
                    sp.dma_start(adj_raw[:, g % LOAD_SLOTS, 0:width], adj[chunk, g, :, 0:width])\
                      .then_inc(adj_loaded[g % LOAD_SLOTS], 16)
                if in_first_pass(q, kind):
                    sp.dma_start(block_of_kept(chunk), adj[chunk, LOADS - 1, :, LOAD - PIECE:LOAD])\
                      .then_inc(kept_loaded, 16)

            def block_of_kept(chunk):
                return adj_kept[:, bass.ds(chunk * PIECE, PIECE)]

            walk(sp, step)

        @block.gpsimd
        def _(pool):
            for n, w in enumerate(weights):
                pool.dma_start(w_raw[:, n, :], w).then_inc(params_loaded, 16)
            for n, b in enumerate(bias_cols):
                pool.dma_start(b_col[:, n:n + 1], b.rearrange("(p a) -> p a", a=1)).then_inc(params_loaded, 16)
            for n, b in enumerate(bias_rows):
                pool.dma_start(b_row[:, n, :], b.partition_broadcast(P)).then_inc(params_loaded, 16)

            def step(q, chunk, src, kind, ended, dst):
                for i in range(PIECES):
                    if is_first(q) and i % 2 == 0:
                        g = i // 2
                        pool.wait_ge(feat_hi_ready, g + 1)
                        pool.tensor_tensor(block_of(feat_lo[0], g), block_of(resid, g),
                                           block_of(feat_hi[0], g).bitcast(F32), ALU.subtract)\
                            .then_inc(feat_lo_ready, 1)
                    if kind in (UV, VU, LAST):
                        for n in range(2):
                            if i == POOL_HID[n]:
                                pool.wait_ge(hid_hi_ready[n], mlps(q))
                                pool.tensor_tensor(hid_lo[:, :], hid[:, :], hid_hi[:, :].bitcast(F32),
                                                   ALU.subtract).then_inc(hid_lo_ready[n], 1)
                    if kind in (GCN, UV, VU) and i == POOL_FEAT:
                        whole = block_of(resid, ended) if kind == GCN else post[:, :]
                        pool.wait_ge(feat_hi_ready, blocks(q))
                        pool.tensor_tensor(block_of(feat_lo[dst], ended), whole,
                                           block_of(feat_hi[dst], ended).bitcast(F32), ALU.subtract)\
                            .then_inc(feat_lo_ready, 1)
                    if chunk is not None and i in POOL_PIECES:
                        pool.wait_ge(adj_hi_ready, q * PIECES + (i + 1))
                        pool.tensor_tensor(adj_lo[:, i % SPLIT_SLOTS, :], raw_piece(chunk, i),
                                           adj_hi[:, i % SPLIT_SLOTS, :].bitcast(F32), ALU.subtract)\
                            .then_inc(adj_lo_by_pool, 1)
                if kind == LAST:
                    pool.wait_ge(normed, norms(q, kind))
                    pool.dma_start(out[ended], block_of(resid, ended)).then_inc(out_written, 16)

            walk(pool, step)
            pool.wait_ge(out_written, 16 * C)

        @block.scalar
        def _(act):
            def step(q, chunk, src, kind, ended, dst):
                for i in range(PIECES):
                    if is_first(q) and i % 2 == 0:
                        g = i // 2
                        act.wait_ge(x_loaded[g], 16)
                        act.activation(block_of(feat_hi[0], g), block_of(resid, g), ACT.Copy)\
                           .then_inc(feat_hi_ready, 1)
                    if is_first(q) and i == PIECES // 2:
                        act.wait_ge(params_loaded, 16 * N_PARAMS)
                        act.activation(w_hi[:, :, :], w_raw[:, :, :], ACT.Copy).then_inc(w_hi_ready, 1)
                    if kind and i == ACT_AGG:
                        act.wait_ge(piece_used, q * PIECES)
                        act.activation(agg_hi[:, :], agg_bank(ended), ACT.Copy).then_inc(agg_hi_ready, 1)
                    if kind in (UV, VU, LAST):
                        for n in range(2):
                            if i == ACT_HID[n]:
                                b = HID_BIAS[kind][n]
                                act.wait_ge(hid_done[n], mlps(q))
                                act.activation(hid_pre[:, :], hid_ps[n][:, :], ACT.Identity, bias=b_col[:, b:b + 1])\
                                   .then_inc(hid_pre_ready[n], 1)
                    if kind in (GCN, LAST) and i == (ACT_STD if kind == GCN else PIECES - 1):
                        act.wait_ge(eps_ready, 1)
                        act.wait_ge(var_ready, norms(q, kind))
                        act.activation(std[:, :], mean_var[:, :, 1], ACT.Sqrt, bias=eps[:, 0:1])\
                           .then_inc(std_ready, 1)
                    if chunk is None:
                        continue
                    if i == PIECES - 1:
                        act.wait_ge(kept_loaded, 16 * (chunk + 1) if in_first_pass(q, kind) else 16 * C)
                    else:
                        g = i // 2
                        act.wait_ge(adj_loaded[g % LOAD_SLOTS],
                                    q * (16 * LOADS // LOAD_SLOTS) + 16 * (g // LOAD_SLOTS + 1))
                    if not is_first(q) or i >= SPLIT_SLOTS:
                        act.wait_ge(piece_used, q * PIECES + (i + 1 - SPLIT_SLOTS))
                    act.activation(adj_hi[:, i % SPLIT_SLOTS, :], raw_piece(chunk, i), ACT.Copy)\
                       .then_inc(adj_hi_ready, 1)

            walk(act, step)

        @block.vector
        def _(dve):
            dve.memset(eps[:, :], EPS).then_inc(eps_ready, 1)

            def leaky_relu(to, of):
                return dve.scalar_tensor_tensor(to[:, :], of[:, :], SLOPE, of[:, :], ALU.mult, ALU.max)

            def statistics(q, kind, ended):
                if kind == GCN:
                    dve.wait_ge(pre_ready, q)
                    dve.scalar_tensor_tensor(summed[:, :], pre[:, :], 0.0, block_of(resid, ended), ALU.max, ALU.add)\
                       .then_inc(sum_ready, 1)
                else:
                    dve.wait_ge(pre_ready, q)
                    leaky_relu(post, pre).then_inc(post_ready, 1)
                    dve.wait_ge(post_ready, mlps(q))
                    dve.tensor_tensor(summed[:, :], post[:, :], block_of(resid, ended), ALU.add)\
                       .then_inc(sum_ready, 1)
                dve.wait_ge(sum_ready, norms(q, kind))
                for j in range(TILES):
                    last = dve.bn_stats(stats[:, j, :], summed[:, j * P:(j + 1) * P])
                last.then_inc(stats_ready, 1)

            def aggregate(q, kind):
                if isinstance(q, int):
                    dve.wait_ge(stats_ready, norms(q, kind))
                for j in range(TILES):
                    last = dve.bn_aggr(mean_var[:, j, :], stats[:, j, :])
                last.then_inc(var_ready, 1)

            def normalise(q, kind, ended):
                dve.wait_ge(std_ready, norms(q, kind))
                dve.reciprocal(rstd[:, :], std[:, :]).then_inc(rstd_ready, 1)
                dve.wait_ge(rstd_ready, norms(q, kind))
                for j in range(TILES):
                    last = dve.tensor_scalar(resid[:, bass.ds(ended * CHUNK + j * P, P)],
                                             summed[:, j * P:(j + 1) * P], mean_var[:, j, 0:1], rstd[:, j:j + 1],
                                             ALU.subtract, ALU.mult)
                last.then_inc(normed, 1)

            def step(q, chunk, src, kind, ended, dst):
                for i in range(PIECES):
                    if is_first(q) and i == PIECES // 2:
                        dve.wait_ge(w_hi_ready, 1)
                        dve.tensor_tensor(w_lo[:, :, :], w_raw[:, :, :], w_hi[:, :, :].bitcast(F32), ALU.subtract)\
                           .then_inc(w_lo_ready, 1)
                    if kind and i == DVE_AGG:
                        dve.wait_ge(agg_hi_ready, q)
                        dve.tensor_tensor(agg_lo[:, :], agg_bank(ended), agg_hi[:, :].bitcast(F32), ALU.subtract)\
                           .then_inc(agg_lo_ready, 1)
                    if kind in (UV, VU, LAST):
                        for n in range(2):
                            if i == DVE_HID[n]:
                                dve.wait_ge(hid_pre_ready[n], mlps(q))
                                leaky_relu(hid, hid_pre).then_inc(hid_ready[n], 1)
                                dve.wait_ge(hid_ready[n], mlps(q))
                                dve.tensor_copy(hid_hi[:, :], hid[:, :]).then_inc(hid_hi_ready[n], 1)
                    if kind and i == (DVE_SUM[GCN] if kind == GCN else DVE_PRE):
                        b = PRE_BIAS[kind]
                        dve.wait_ge(pre_done, q)
                        dve.tensor_tensor(by_tile(pre[:, :]), by_tile(pre_ps[:, :]),
                                          b_row[:, b:b + 1, :].to_broadcast([P, TILES, P]), ALU.add)\
                           .then_inc(pre_ready, 1)
                    if kind in (GCN, LAST) and i == DVE_SUM[kind]:
                        statistics(q, kind, ended)
                    if kind in (GCN, LAST) and i == DVE_SUM[kind] + 1:
                        aggregate(q, kind)
                    if kind in (GCN, LAST) and i == DVE_NORM[kind]:
                        normalise(q, kind, ended)
                    if kind == GCN and i == DVE_NORM[kind]:
                        dve.wait_ge(normed, norms(q, kind))
                        dve.tensor_copy(block_of(feat_hi[dst], ended), block_of(resid, ended))\
                           .then_inc(feat_hi_ready, 1)
                    if kind in (UV, VU) and i == DVE_FEAT:
                        dve.wait_ge(pre_ready, q)
                        leaky_relu(post, pre).then_inc(post_ready, 1)
                        dve.wait_ge(post_ready, mlps(q))
                        dve.tensor_copy(block_of(feat_hi[dst], ended), post[:, :]).then_inc(feat_hi_ready, 1)
                    if chunk is not None and i in DVE_PIECES:
                        if kind in (GCN, LAST) and i == DVE_SUM[kind]:
                            dve.wait_ge(stats_ready, norms(q, kind))
                        dve.wait_ge(adj_hi_ready, q * PIECES + (i + 1))
                        dve.tensor_tensor(adj_lo[:, i % SPLIT_SLOTS, :], raw_piece(chunk, i),
                                          adj_hi[:, i % SPLIT_SLOTS, :].bitcast(F32), ALU.subtract)\
                           .then_inc(adj_lo_by_dve, 1)

            walk(dve, step)

        @block.tensor
        def _(pe):
            def product(to, left, right, start=True, stop=True):
                (l_hi, l_lo), (r_hi, r_lo) = left, right
                pe.matmul(to, l_hi, r_hi, start=start, stop=False)
                pe.matmul(to, l_hi, r_lo, start=False, stop=False)
                return pe.matmul(to, l_lo, r_hi, start=False, stop=stop)

            def hidden(n, w, hi, lo):
                product(hid_ps[n][:, :], (w_hi[:, w, :], w_lo[:, w, :]), (hi[:, :], lo[:, :]))\
                    .then_inc(hid_done[n], 1)

            def last_layer(w, hi, lo):
                for j in range(TILES):
                    own = slice(j * P, (j + 1) * P)
                    last = product(pre_ps[:, own], (hi[:, own], lo[:, own]), (w_hi[:, w, :], w_lo[:, w, :]))
                last.then_inc(pre_done, 1)

            def step(q, chunk, src, kind, ended, dst):
                bank = agg_bank(chunk) if chunk is not None else None
                for i in range(PIECES):
                    if is_first(q) and i == PIECES - 1:
                        pe.wait_ge(w_lo_ready, 1)
                    if kind == GCN and i == PE_GCN:
                        pe.wait_ge(agg_lo_ready, q)
                        last_layer(LAYERS[kind][0], agg_hi, agg_lo)
                    if kind in (UV, VU, LAST):
                        if i == PE_LAYER[0]:
                            pe.wait_ge(agg_lo_ready, q)
                            hidden(0, LAYERS[kind][0], agg_hi, agg_lo)
                        if i == PE_LAYER[1]:
                            pe.wait_ge(hid_lo_ready[0], mlps(q))
                            hidden(1, LAYERS[kind][1], hid_hi, hid_lo)
                        if i == PE_LAYER[2]:
                            pe.wait_ge(hid_lo_ready[1], mlps(q))
                            last_layer(LAYERS[kind][2], hid_hi, hid_lo)
                    if chunk is None:
                        continue
                    if isinstance(chunk, int) and i % 2 == 0:
                        pe.wait_ge(feat_hi_ready, q + (i // 2 + 1))
                        pe.wait_ge(feat_lo_ready, q + (i // 2 + 1))
                    pieces, ready = ((POOL_PIECES, adj_lo_by_pool) if i in POOL_PIECES
                                     else (DVE_PIECES, adj_lo_by_dve))
                    pe.wait_ge(ready, q * len(pieces) + lo_counts(pieces, i))
                    for k in range(PIECE // CHUNK):
                        tile = i * (PIECE // CHUNK) + k
                        own, cols = slice(tile * P, (tile + 1) * P), slice(k * CHUNK, (k + 1) * CHUNK)
                        last = product(bank, (feat_hi[src][:, own], feat_lo[src][:, own]),
                                       (adj_hi[:, i % SPLIT_SLOTS, cols], adj_lo[:, i % SPLIT_SLOTS, cols]),
                                       start=tile == 0, stop=tile == C * TILES - 1)
                    last.then_inc(piece_used, 1)

            walk(pe, step)


def kernel(x, adj, L0_gnn_kernel, L0_gnn_bias, **mlps):
    import numpy as _np
    import concourse.bacc as _bacc
    from concourse.bass_utils import run_bass_kernel_spmd as _run

    nodes, features = x.shape
    chunks = nodes // CHUNK
    node = (chunks, P, TILES)
    arrays = {"x": _np.ascontiguousarray(x).reshape(chunks, P, TILES * features)}
    arrays["adj"] = _np.ascontiguousarray(
        _np.asarray(adj).reshape(node + node).transpose(0, 3, 4, 5, 2, 1)).reshape(chunks, chunks, P, TILES * CHUNK)
    arrays["gcn_w"] = _np.ascontiguousarray(L0_gnn_kernel)
    arrays["gcn_b"] = _np.ascontiguousarray(L0_gnn_bias)
    for tag in ("uv", "vu"):
        for part in ("W1", "b1", "W2", "b2", "W3", "b3"):
            arrays[f"{tag}_{part}"] = _np.ascontiguousarray(mlps[f"L1_gnn_{tag}_{part}"])

    nc = _bacc.Bacc("TRN2", target_bir_lowering=False, num_devices=1)
    aps = {name: nc.dram_tensor(f"in_{name}", a.shape, mybir.dt.from_np(a.dtype), kind="ExternalInput").ap()
           for name, a in arrays.items()}
    out = nc.dram_tensor("out", arrays["x"].shape, F32, kind="ExternalOutput").ap()
    uv, vu = ({part: aps[f"{tag}_{part}"] for part in ("W1", "b1", "W2", "b2", "W3", "b3")} for tag in ("uv", "vu"))
    gnn_kernel(nc, aps["x"], aps["adj"], aps["gcn_w"], aps["gcn_b"], uv, vu, out)
    ran = _run(nc, [{f"in_{name}": a for name, a in arrays.items()}], core_ids=[0])
    return ran.results[0]["out"].reshape(nodes, features)
```

```python
import concourse.bass as bass
from concourse import mybir
from contextlib import ExitStack

F32 = mybir.dt.float32
F32R = mybir.dt.float32r
ALU = mybir.AluOpType
ACT = mybir.ActivationFunctionType

P = 128
CHUNK = 512
TILES = CHUNK // P
EPS = 1e-5
SLOPE = 0.01

PIECE = 2 * CHUNK
KEPT = 2
LOAD_SLOTS = 7
SPLIT_SLOTS = 4
LAST_PARTS = 2

PE_LAYER = (2, 6, 9)
PE_GCN = 2
ACT_AGG, ACT_HID = 3, (6, 9)
ACT_STD = {"gcn": 11, "last": 16}
DVE_AGG, DVE_HID = 3, (6, 9)
DVE_PRE = {"gcn": 6, "uv": 11, "vu": 11, "last": 11}
DVE_LEAKY = 12
DVE_STATS = {"gcn": 6, "last": 14}
DVE_FEAT = 13
DVE_NORM = {"gcn": 11, "last": 16}
POOL_HID, POOL_SUM, POOL_FEAT = 7, 13, 13
POOL_PIECES = (4, 8, 11)


def gnn_kernel(nc, x, adj, gcn_w, gcn_b, uv, vu, out):
    C = x.shape[0]
    PIECES = adj.shape[1]
    LOADS = PIECES - KEPT
    DVE_PIECES = tuple(i for i in range(PIECES) if i not in POOL_PIECES)
    assert PIECES * PIECE == C * TILES * CHUNK and LOADS == 2 * LOAD_SLOTS and PIECES % SPLIT_SLOTS == 0

    GCN, UV, VU, LAST = "gcn", "uv", "vu", "last"
    PASSES = 6
    weights = [uv["W1"], uv["W2"], vu["W1"], vu["W2"], gcn_w, uv["W3"], vu["W3"]]
    LAYERS = {GCN: (4,), UV: (0, 1, 5), VU: (2, 3, 6), LAST: (0, 1, 5)}
    N_SPLIT = 4
    bias_cols = [uv["b1"], uv["b2"], vu["b1"], vu["b2"]]
    HID_BIAS = {UV: (0, 1), VU: (2, 3), LAST: (0, 1)}
    bias_rows = [gcn_b, uv["b3"], vu["b3"]]
    PRE_BIAS = {GCN: 0, UV: 1, VU: 2, LAST: 1}
    N_W = len(weights)
    N_PARAMS = N_W + len(bias_cols) + len(bias_rows)

    ctx = ExitStack()
    with ctx:
        def sb(name, shape, dt=F32):
            return ctx.enter_context(nc.sbuf_tensor(name, shape, dt))

        def ps(name, shape):
            return ctx.enter_context(nc.psum_tensor(name, shape, F32))

        def sem(name):
            return ctx.enter_context(nc.semaphore(name))

        adj_raw = sb("adj_raw", [P, LOAD_SLOTS, PIECE])
        adj_kept = sb("adj_kept", [P, C * KEPT * PIECE])
        adj_hi = sb("adj_hi", [P, SPLIT_SLOTS, PIECE], F32R)
        adj_lo = sb("adj_lo", [P, SPLIT_SLOTS, PIECE], F32R)
        feat_hi = [sb(f"feat_hi{b}", [P, C * CHUNK], F32R) for b in range(2)]
        feat_lo = [sb(f"feat_lo{b}", [P, C * CHUNK], F32R) for b in range(2)]
        resid = sb("resid", [P, C * CHUNK])
        w_raw = sb("w_raw", [P, N_W, P])
        w_hi = sb("w_hi", [P, N_SPLIT, P], F32R)
        w_lo = sb("w_lo", [P, N_SPLIT, P], F32R)
        b_col = sb("b_col", [P, len(bias_cols)])
        b_row = sb("b_row", [P, len(bias_rows), P])
        hid = sb("hid", [P, CHUNK])
        in_hi = sb("in_hi", [P, CHUNK], F32R)
        in_lo = sb("in_lo", [P, CHUNK], F32R)
        pre = sb("pre", [P, CHUNK])
        stats = sb("stats", [P, TILES, 6])
        mean_var = sb("mean_var", [P, TILES, 2])
        std = sb("std", [P, TILES])
        rstd = sb("rstd", [P, TILES])
        eps = sb("eps", [P, 1])

        agg_ps = ps("agg_ps", [P, 2 * CHUNK])
        hid_ps = [ps(f"hid_ps{n}", [P, LAST_PARTS * CHUNK]) for n in range(2)]
        pre_ps = ps("pre_ps", [P, LAST_PARTS * CHUNK])

        x_loaded = [sem(f"x_loaded{g}") for g in range(C)]
        adj_loaded = [sem(f"adj_loaded{s}") for s in range(LOAD_SLOTS)]
        kept_loaded = [sem(f"kept_loaded{k}") for k in range(KEPT)]
        params_loaded = sem("params_loaded")
        eps_ready = sem("eps_ready")
        w_hi_ready = sem("w_hi_ready")
        w_lo_ready = sem("w_lo_ready")
        adj_hi_ready = sem("adj_hi_ready")
        adj_lo_by_dve = sem("adj_lo_by_dve")
        adj_lo_by_pool = sem("adj_lo_by_pool")
        piece_used = sem("piece_used")
        feat_hi_ready = sem("feat_hi_ready")
        feat_lo_ready = sem("feat_lo_ready")
        agg_hi_ready = sem("agg_hi_ready")
        agg_lo_ready = sem("agg_lo_ready")
        hid_done = [sem(f"hid_done{n}") for n in range(2)]
        hid_pre_ready = [sem(f"hid_pre_ready{n}") for n in range(2)]
        hid_ready = [sem(f"hid_ready{n}") for n in range(2)]
        hid_hi_ready = sem("hid_hi_ready")
        hid_lo_ready = sem("hid_lo_ready")
        pre_done = sem("pre_done")
        pre_ready = sem("pre_ready")
        post_ready = sem("post_ready")
        sum_ready = sem("sum_ready")
        stats_ready = sem("stats_ready")
        var_ready = sem("var_ready")
        std_ready = sem("std_ready")
        rstd_ready = sem("rstd_ready")
        normed = sem("normed")
        out_written = sem("out_written")

        def block_of(t, chunk):
            return t[:, bass.ds(chunk * CHUNK, CHUNK)]

        def by_tile(ap):
            return ap.rearrange("p (j f) -> p j f", f=P)

        def raw_piece(chunk, i):
            if i >= LOADS:
                return adj_kept[:, bass.ds((chunk * KEPT + (i - LOADS)) * PIECE, PIECE)]
            return adj_raw[:, i % LOAD_SLOTS, :]

        def agg_bank(chunk, own=slice(0, TILES)):
            return agg_ps[:, bass.ds((chunk % 2) * CHUNK + own.start * P, (own.stop - own.start) * P)]

        def resid_block(chunk, own=slice(0, TILES)):
            return resid[:, bass.ds(chunk * CHUNK + own.start * P, (own.stop - own.start) * P)]

        def walk(eng, step):
            step(0, 0, 0, None, None, None)
            with eng.Fori(1, C) as c:
                step(c, c, 0, GCN, c - 1, 1)
            step(C, 0, 1, GCN, C - 1, 1)
            with eng.Fori(C, C * (PASSES - 1), 2 * C) as q0:
                with eng.Fori(1, C) as c:
                    step(q0 + c, c, 1, UV, c - 1, 0)
                step(q0 + C, 0, 0, UV, C - 1, 0)
                with eng.Fori(1, C) as c:
                    step(q0 + C + c, c, 0, VU, c - 1, 1)
                step(q0 + 2 * C, 0, 1, VU, C - 1, 1)
            with eng.Fori(1, C) as c:
                step(C * (PASSES - 1) + c, c, 1, LAST, c - 1, None)
            step(C * PASSES, None, None, LAST, C - 1, None)

        def is_first(q):
            return isinstance(q, int) and q == 0

        def in_first_pass(q, kind):
            return is_first(q) or (kind == GCN and not isinstance(q, int))

        def mlps(q):
            return q - C

        def blocks(q):
            return q + C

        def norms(q, kind):
            return q if kind == GCN else q - C * (PASSES - 2)

        def parts(chunk):
            n = LAST_PARTS if chunk is None else 1
            return [(k, slice(k * TILES // n, (k + 1) * TILES // n)) for k in range(n)]

        def cols(own):
            return slice(own.start * P, own.stop * P)

        def ps_cols(k, own):
            return slice(k * CHUNK + own.start * P, k * CHUNK + own.stop * P)

        def lo_counts(pieces, last):
            return sum(i <= last for i in pieces)

        block = ctx.enter_context(nc.Block())

        @block.sync
        def _(sp):
            def wait_split(q, last):
                by_dve = q * len(DVE_PIECES) + lo_counts(DVE_PIECES, last)
                by_pool = q * len(POOL_PIECES) + lo_counts(POOL_PIECES, last)
                if not isinstance(q, int):
                    by_dve, by_pool = sp.snap(sp.to_reg(by_dve)), sp.snap(sp.to_reg(by_pool))
                sp.wait_ge(adj_lo_by_dve, by_dve)
                if not is_first(q) or by_pool:
                    sp.wait_ge(adj_lo_by_pool, by_pool)

            def load_x(g):
                sp.dma_start(block_of(resid, g), x[g]).then_inc(x_loaded[g], 16)

            def load_params():
                for n, w in enumerate(weights):
                    sp.dma_start(w_raw[:, n, :], w).then_inc(params_loaded, 16)
                for n, b in enumerate(bias_cols):
                    sp.dma_start(b_col[:, n:n + 1], b.rearrange("(p a) -> p a", a=1)).then_inc(params_loaded, 16)
                for n, b in enumerate(bias_rows):
                    sp.dma_start(b_row[:, n, :], b.partition_broadcast(P)).then_inc(params_loaded, 16)

            def step(q, chunk, src, kind, ended, dst):
                if chunk is None:
                    sp.wait_ge(normed, norms(q, kind) - 1)
                    sp.dma_start(out[0:C - 1].rearrange("c p n -> p c n"),
                                 resid[:, 0:(C - 1) * CHUNK].rearrange("p (c n) -> p c n", c=C - 1))\
                      .then_inc(out_written, 16)
                    for k, own in parts(chunk):
                        sp.wait_ge(normed, norms(q, kind) + k)
                        sp.dma_start(out[ended][:, cols(own)], resid_block(ended, own)).then_inc(out_written, 16)
                    sp.wait_ge(out_written, 16 * (1 + LAST_PARTS))
                    return
                for i in range(LOADS):
                    if is_first(q) and i % 2 == 0:
                        load_x(i // 2)
                    if i >= LOAD_SLOTS:
                        wait_split(q, i - LOAD_SLOTS)
                    elif not is_first(q):
                        wait_split(q - 1, i - LOAD_SLOTS + LOADS)
                    sp.dma_start(adj_raw[:, i % LOAD_SLOTS, :], adj[chunk, i])\
                      .then_inc(adj_loaded[i % LOAD_SLOTS], 16)
                    if is_first(q) and i == LOAD_SLOTS - 1:
                        load_params()
                if is_first(q):
                    load_x(LOADS // 2)
                if in_first_pass(q, kind):
                    for k in range(KEPT):
                        sp.dma_start(raw_piece(chunk, LOADS + k), adj[chunk, LOADS + k]).then_inc(kept_loaded[k], 16)

            walk(sp, step)

        @block.gpsimd
        def _(pool):
            def step(q, chunk, src, kind, ended, dst):
                for i in range(PIECES + 1):
                    if is_first(q) and i % 2 == 0 and i < PIECES:
                        g = i // 2
                        pool.wait_ge(feat_hi_ready, g + 1)
                        pool.tensor_tensor(block_of(feat_lo[0], g), block_of(resid, g),
                                           block_of(feat_hi[0], g).bitcast(F32), ALU.subtract)\
                            .then_inc(feat_lo_ready, 1)
                    if kind in (UV, VU, LAST) and i == POOL_HID:
                        for k, own in parts(chunk):
                            pool.wait_ge(hid_hi_ready, mlps(q) + k)
                            pool.tensor_tensor(in_lo[:, cols(own)], hid[:, cols(own)],
                                               in_hi[:, cols(own)].bitcast(F32), ALU.subtract)\
                                .then_inc(hid_lo_ready, 1)
                    if kind == LAST and i == POOL_SUM:
                        for k, own in parts(chunk):
                            pool.wait_ge(post_ready, mlps(q) + k)
                            pool.tensor_tensor(pre[:, cols(own)], pre[:, cols(own)], resid_block(ended, own), ALU.add)\
                                .then_inc(sum_ready, 1)
                    if kind in (GCN, UV, VU) and i == POOL_FEAT:
                        whole = block_of(resid, ended) if kind == GCN else pre[:, :]
                        pool.wait_ge(feat_hi_ready, blocks(q))
                        pool.tensor_tensor(block_of(feat_lo[dst], ended), whole,
                                           block_of(feat_hi[dst], ended).bitcast(F32), ALU.subtract)\
                            .then_inc(feat_lo_ready, 1)
                    if chunk is not None and i in POOL_PIECES:
                        pool.wait_ge(adj_hi_ready, q * PIECES + (i + 1))
                        pool.tensor_tensor(adj_lo[:, i % SPLIT_SLOTS, :], raw_piece(chunk, i),
                                           adj_hi[:, i % SPLIT_SLOTS, :].bitcast(F32), ALU.subtract)\
                            .then_inc(adj_lo_by_pool, 1)

            walk(pool, step)

        @block.scalar
        def _(act):
            def step(q, chunk, src, kind, ended, dst):
                for i in range(PIECES + 1):
                    if is_first(q) and i % 2 == 0 and i < PIECES:
                        g = i // 2
                        act.wait_ge(x_loaded[g], 16)
                        act.activation(block_of(feat_hi[0], g), block_of(resid, g), ACT.Copy)\
                           .then_inc(feat_hi_ready, 1)
                    if is_first(q) and i == PIECES // 2:
                        act.wait_ge(params_loaded, 16 * N_PARAMS)
                        act.activation(w_hi[:, :, :], w_raw[:, 0:N_SPLIT, :], ACT.Copy).then_inc(w_hi_ready, 1)
                    if kind and i == ACT_AGG:
                        act.wait_ge(piece_used, q * PIECES)
                        to = hid if kind == GCN else in_hi
                        for k, own in parts(chunk):
                            act.activation(to[:, cols(own)], agg_bank(ended, own), ACT.Copy)\
                               .then_inc(agg_hi_ready, 1)
                    if kind in (UV, VU, LAST):
                        for n in range(2):
                            if i == ACT_HID[n]:
                                b = HID_BIAS[kind][n]
                                for k, own in parts(chunk):
                                    act.wait_ge(hid_done[n], mlps(q) + k)
                                    act.activation(hid[:, cols(own)], hid_ps[n][:, ps_cols(k, own)], ACT.Identity,
                                                   bias=b_col[:, b:b + 1]).then_inc(hid_pre_ready[n], 1)
                    if kind in (GCN, LAST) and i == ACT_STD[kind]:
                        act.wait_ge(eps_ready, 1)
                        for k, own in parts(chunk):
                            act.wait_ge(var_ready, norms(q, kind) + k)
                            act.activation(std[:, own], mean_var[:, own, 1], ACT.Sqrt, bias=eps[:, 0:1])\
                               .then_inc(std_ready, 1)
                    if chunk is None or i == PIECES:
                        continue
                    if i >= LOADS:
                        loaded = chunk + 1 if in_first_pass(q, kind) else C
                        act.wait_ge(kept_loaded[i - LOADS], 16 * loaded)
                    else:
                        act.wait_ge(adj_loaded[i % LOAD_SLOTS],
                                    q * (16 * LOADS // LOAD_SLOTS) + 16 * (i // LOAD_SLOTS + 1))
                    if not is_first(q) or i >= SPLIT_SLOTS:
                        act.wait_ge(piece_used, q * PIECES + (i + 1 - SPLIT_SLOTS))
                    act.activation(adj_hi[:, i % SPLIT_SLOTS, :], raw_piece(chunk, i), ACT.Copy)\
                       .then_inc(adj_hi_ready, 1)


            walk(act, step)

        @block.vector
        def _(dve):
            dve.memset(eps[:, :], EPS).then_inc(eps_ready, 1)

            def leaky_relu(t, own):
                t = t[:, cols(own)]
                return dve.scalar_tensor_tensor(t, t, SLOPE, t, ALU.mult, ALU.max)

            def statistics(q, kind, ended, k, own):
                if kind == GCN:
                    dve.wait_ge(pre_ready, q + k)
                    dve.scalar_tensor_tensor(pre[:, cols(own)], pre[:, cols(own)], 0.0, resid_block(ended, own),
                                             ALU.max, ALU.add).then_inc(sum_ready, 1)
                dve.wait_ge(sum_ready, norms(q, kind) + k)
                for j in range(own.start, own.stop):
                    last = dve.bn_stats(stats[:, j, :], pre[:, j * P:(j + 1) * P])
                last.then_inc(stats_ready, 1)

            def aggregate(q, kind, k, own):
                if isinstance(q, int):
                    dve.wait_ge(stats_ready, norms(q, kind) + k)
                for j in range(own.start, own.stop):
                    last = dve.bn_aggr(mean_var[:, j, :], stats[:, j, :])
                last.then_inc(var_ready, 1)

            def normalise(q, kind, ended, k, own):
                dve.wait_ge(std_ready, norms(q, kind) + k)
                dve.reciprocal(rstd[:, own], std[:, own]).then_inc(rstd_ready, 1)
                dve.wait_ge(rstd_ready, norms(q, kind) + k)
                for j in range(own.start, own.stop):
                    last = dve.tensor_scalar(resid_block(ended, slice(j, j + 1)), pre[:, j * P:(j + 1) * P],
                                             mean_var[:, j, 0:1], rstd[:, j:j + 1], ALU.subtract, ALU.mult)
                last.then_inc(normed, 1)

            def step(q, chunk, src, kind, ended, dst):
                for i in range(PIECES + 1):
                    if is_first(q) and i == PIECES // 2:
                        dve.wait_ge(w_hi_ready, 1)
                        dve.tensor_tensor(w_lo[:, :, :], w_raw[:, 0:N_SPLIT, :], w_hi[:, :, :].bitcast(F32), ALU.subtract)\
                           .then_inc(w_lo_ready, 1)
                    if kind in (UV, VU, LAST) and i == DVE_AGG:
                        for k, own in parts(chunk):
                            dve.wait_ge(agg_hi_ready, q + len(parts(chunk)) - 1)
                            dve.tensor_tensor(in_lo[:, cols(own)], agg_bank(ended, own),
                                              in_hi[:, cols(own)].bitcast(F32), ALU.subtract)\
                               .then_inc(agg_lo_ready, 1)
                    if kind in (UV, VU, LAST):
                        for n in range(2):
                            if i == DVE_HID[n]:
                                for k, own in parts(chunk):
                                    dve.wait_ge(hid_pre_ready[n], mlps(q) + k)
                                    leaky_relu(hid, own).then_inc(hid_ready[n], 1)
                                    if n == 0:
                                        dve.wait_ge(hid_ready[0], mlps(q) + k)
                                        dve.tensor_copy(in_hi[:, cols(own)], hid[:, cols(own)])\
                                           .then_inc(hid_hi_ready, 1)
                    if kind and i == DVE_PRE[kind]:
                        b = PRE_BIAS[kind]
                        for k, own in parts(chunk):
                            n_own = own.stop - own.start
                            dve.wait_ge(pre_done, q + k)
                            dve.tensor_tensor(by_tile(pre[:, cols(own)]), by_tile(pre_ps[:, ps_cols(k, own)]),
                                              b_row[:, b:b + 1, :].to_broadcast([P, n_own, P]), ALU.add)\
                               .then_inc(pre_ready, 1)
                    if kind in (GCN, LAST) and i == DVE_STATS[kind]:
                        for k, own in parts(chunk):
                            statistics(q, kind, ended, k, own)
                    if kind in (GCN, LAST) and i == DVE_STATS[kind] + 1:
                        for k, own in parts(chunk):
                            aggregate(q, kind, k, own)
                    if kind in (GCN, LAST) and i == DVE_NORM[kind]:
                        for k, own in parts(chunk):
                            normalise(q, kind, ended, k, own)
                    if kind == GCN and i == DVE_NORM[kind]:
                        dve.wait_ge(normed, norms(q, kind))
                        dve.tensor_copy(block_of(feat_hi[dst], ended), block_of(resid, ended))\
                           .then_inc(feat_hi_ready, 1)
                    if kind in (UV, VU, LAST) and i == DVE_LEAKY:
                        for k, own in parts(chunk):
                            dve.wait_ge(pre_ready, q + k)
                            leaky_relu(pre, own).then_inc(post_ready, 1)
                    if kind in (UV, VU) and i == DVE_FEAT:
                        dve.wait_ge(post_ready, mlps(q))
                        dve.tensor_copy(block_of(feat_hi[dst], ended), pre[:, :]).then_inc(feat_hi_ready, 1)
                    if chunk is not None and i in DVE_PIECES:
                        if kind in (GCN, LAST) and i == DVE_STATS[kind]:
                            dve.wait_ge(stats_ready, norms(q, kind))
                        dve.wait_ge(adj_hi_ready, q * PIECES + (i + 1))
                        dve.tensor_tensor(adj_lo[:, i % SPLIT_SLOTS, :], raw_piece(chunk, i),
                                          adj_hi[:, i % SPLIT_SLOTS, :].bitcast(F32), ALU.subtract)\
                           .then_inc(adj_lo_by_dve, 1)

            walk(dve, step)

        @block.tensor
        def _(pe):
            def product(to, left, right, start=True, stop=True):
                (l_hi, l_lo), (r_hi, r_lo) = left, right
                pe.matmul(to, l_hi, r_hi, start=start, stop=False)
                pe.matmul(to, l_hi, r_lo, start=False, stop=False)
                return pe.matmul(to, l_lo, r_hi, start=False, stop=stop)

            def hidden(n, w, k, own):
                product(hid_ps[n][:, ps_cols(k, own)], (w_hi[:, w, :], w_lo[:, w, :]), (in_hi[:, cols(own)], in_lo[:, cols(own)]))\
                    .then_inc(hid_done[n], 1)

            def last_layer(w, k, own):
                for j in range(own.start, own.stop):
                    last = pe.matmul(pre_ps[:, ps_cols(k, slice(j, j + 1))], hid[:, j * P:(j + 1) * P], w_raw[:, w, :],
                                     start=True, stop=True)
                last.then_inc(pre_done, 1)

            def step(q, chunk, src, kind, ended, dst):
                bank = agg_bank(chunk) if chunk is not None else None
                for i in range(PIECES + 1):
                    if is_first(q) and i == PIECES - 1:
                        pe.wait_ge(w_lo_ready, 1)
                    for k, own in parts(chunk):
                        if kind == GCN and i == PE_GCN:
                            pe.wait_ge(agg_hi_ready, q)
                            last_layer(LAYERS[kind][0], k, own)
                        if kind in (UV, VU, LAST):
                            if i == PE_LAYER[0]:
                                pe.wait_ge(agg_lo_ready, mlps(q) + k)
                                hidden(0, LAYERS[kind][0], k, own)
                            if i == PE_LAYER[1]:
                                pe.wait_ge(hid_lo_ready, mlps(q) + k)
                                hidden(1, LAYERS[kind][1], k, own)
                            if i == PE_LAYER[2]:
                                pe.wait_ge(hid_ready[1], mlps(q) + k)
                                last_layer(LAYERS[kind][2], k, own)
                    if chunk is None or i == PIECES:
                        continue
                    if isinstance(chunk, int) and i % 2 == 0:
                        pe.wait_ge(feat_hi_ready, q + (i // 2 + 1))
                        pe.wait_ge(feat_lo_ready, q + (i // 2 + 1))
                    pieces, ready = ((POOL_PIECES, adj_lo_by_pool) if i in POOL_PIECES
                                     else (DVE_PIECES, adj_lo_by_dve))
                    pe.wait_ge(ready, q * len(pieces) + lo_counts(pieces, i))
                    for k in range(PIECE // CHUNK):
                        tile = i * (PIECE // CHUNK) + k
                        own, piece_cols = slice(tile * P, (tile + 1) * P), slice(k * CHUNK, (k + 1) * CHUNK)
                        last = product(bank, (feat_hi[src][:, own], feat_lo[src][:, own]),
                                       (adj_hi[:, i % SPLIT_SLOTS, piece_cols], adj_lo[:, i % SPLIT_SLOTS, piece_cols]),
                                       start=tile == 0, stop=tile == C * TILES - 1)
                    last.then_inc(piece_used, 1)

            walk(pe, step)


def kernel(x, adj, L0_gnn_kernel, L0_gnn_bias, **mlps):
    import numpy as _np
    import concourse.bacc as _bacc
    from concourse.bass_utils import run_bass_kernel_spmd as _run

    nodes, features = x.shape
    chunks = nodes // CHUNK
    node = (chunks, P, TILES)
    arrays = {"x": _np.ascontiguousarray(x).reshape(chunks, P, TILES * features)}
    tiles = PIECE // CHUNK
    to_from = _np.asarray(adj).reshape(node + (chunks, P, TILES // tiles, tiles))
    arrays["adj"] = _np.ascontiguousarray(to_from.transpose(0, 3, 5, 4, 6, 2, 1))\
        .reshape(chunks, chunks * TILES // tiles, P, PIECE)
    arrays["gcn_w"] = _np.ascontiguousarray(L0_gnn_kernel)
    arrays["gcn_b"] = _np.ascontiguousarray(L0_gnn_bias)
    for tag in ("uv", "vu"):
        for part in ("W1", "b1", "W2", "b2", "W3", "b3"):
            arrays[f"{tag}_{part}"] = _np.ascontiguousarray(mlps[f"L1_gnn_{tag}_{part}"])

    nc = _bacc.Bacc("TRN2", target_bir_lowering=False, num_devices=1, dynamic_dma_scratch_size=1024)
    aps = {name: nc.dram_tensor(f"in_{name}", a.shape, mybir.dt.from_np(a.dtype), kind="ExternalInput").ap()
           for name, a in arrays.items()}
    out = nc.dram_tensor("out", arrays["x"].shape, F32, kind="ExternalOutput").ap()
    uv, vu = ({part: aps[f"{tag}_{part}"] for part in ("W1", "b1", "W2", "b2", "W3", "b3")} for tag in ("uv", "vu"))
    gnn_kernel(nc, aps["x"], aps["adj"], aps["gcn_w"], aps["gcn_b"], uv, vu, out)
    ran = _run(nc, [{f"in_{name}": a for name, a in arrays.items()}], core_ids=[0])
    return ran.results[0]["out"].reshape(nodes, features)
```

```python
import concourse.bass as bass
from concourse import mybir
from contextlib import ExitStack

F32 = mybir.dt.float32
F32R = mybir.dt.float32r
ALU = mybir.AluOpType
ACT = mybir.ActivationFunctionType

P = 128
CHUNK = 512
TILES = CHUNK // P
EPS = 1e-5
SLOPE = 0.01

PIECE = CHUNK
LOAD = 2
KEPT = 2
LOAD_SLOTS = 7
SPLIT_SLOTS = 8
LAST_PARTS = 2

PE_LAYER = (4, 12, 16)
PE_GCN = 3
ACT_AGG, ACT_HID = 7, (13, 20)
ACT_STD = {"gcn": 19, "last": 30}
DVE_AGG, DVE_HID = 5, (12, 19)
DVE_PRE = {"gcn": 12, "uv": 24, "vu": 24, "last": 24}
DVE_LEAKY = 24
DVE_STATS = {"gcn": 15, "last": 27}
DVE_FEAT = 25
DVE_NORM = {"gcn": 20, "last": 31}
POOL_HID, POOL_SUM, POOL_FEAT = 13, 22, 22
POOL_PIECES = (3, 9, 13, 18, 20, 31)


def gnn_kernel(nc, x, adj, gcn_w, gcn_b, uv, vu, out):
    C = x.shape[0]
    PIECES = adj.shape[1] * LOAD
    LOADS = adj.shape[1] - KEPT
    DVE_PIECES = tuple(i for i in range(PIECES) if i not in POOL_PIECES)
    assert PIECES == C * TILES and LOADS == 2 * LOAD_SLOTS and PIECES % SPLIT_SLOTS == 0
    assert all(i in DVE_PIECES for i in DVE_STATS.values())

    GCN, UV, VU, LAST = "gcn", "uv", "vu", "last"
    PASSES = 6
    weights = [uv["W1"], uv["W2"], vu["W1"], vu["W2"], gcn_w, uv["W3"], vu["W3"]]
    LAYERS = {GCN: (4,), UV: (0, 1, 5), VU: (2, 3, 6), LAST: (0, 1, 5)}
    N_SPLIT = 4
    bias_cols = [uv["b1"], uv["b2"], vu["b1"], vu["b2"]]
    HID_BIAS = {UV: (0, 1), VU: (2, 3), LAST: (0, 1)}
    bias_rows = [gcn_b, uv["b3"], vu["b3"]]
    PRE_BIAS = {GCN: 0, UV: 1, VU: 2, LAST: 1}
    N_W = len(weights)
    N_PARAMS = N_W + len(bias_cols) + len(bias_rows)

    ctx = ExitStack()
    with ctx:
        def sb(name, shape, dt=F32):
            return ctx.enter_context(nc.sbuf_tensor(name, shape, dt))

        def ps(name, shape):
            return ctx.enter_context(nc.psum_tensor(name, shape, F32))

        def sem(name):
            return ctx.enter_context(nc.semaphore(name))

        adj_raw = sb("adj_raw", [P, LOAD_SLOTS, LOAD * PIECE])
        adj_kept = sb("adj_kept", [P, C * KEPT * LOAD * PIECE])
        adj_hi = sb("adj_hi", [P, SPLIT_SLOTS, PIECE], F32R)
        adj_lo = sb("adj_lo", [P, SPLIT_SLOTS, PIECE], F32R)
        feat_hi = [sb(f"feat_hi{b}", [P, C * CHUNK], F32R) for b in range(2)]
        feat_lo = [sb(f"feat_lo{b}", [P, C * CHUNK], F32R) for b in range(2)]
        resid = sb("resid", [P, C * CHUNK])
        w_raw = sb("w_raw", [P, N_W, P])
        w_hi = sb("w_hi", [P, N_SPLIT, P], F32R)
        w_lo = sb("w_lo", [P, N_SPLIT, P], F32R)
        b_col = sb("b_col", [P, len(bias_cols)])
        b_row = sb("b_row", [P, len(bias_rows), P])
        hid = sb("hid", [P, CHUNK])
        in_hi = sb("in_hi", [P, CHUNK], F32R)
        in_lo = sb("in_lo", [P, CHUNK], F32R)
        pre = sb("pre", [P, CHUNK])
        stats = sb("stats", [P, TILES, 6])
        mean_var = sb("mean_var", [P, TILES, 2])
        std = sb("std", [P, TILES])
        rstd = sb("rstd", [P, TILES])
        eps = sb("eps", [P, 1])

        agg_ps = ps("agg_ps", [P, 2 * CHUNK])
        hid_ps = [ps(f"hid_ps{n}", [P, LAST_PARTS * CHUNK]) for n in range(2)]
        pre_ps = ps("pre_ps", [P, LAST_PARTS * CHUNK])

        x_loaded = [sem(f"x_loaded{g}") for g in range(C)]
        adj_loaded = [sem(f"adj_loaded{s}") for s in range(LOAD_SLOTS)]
        kept_loaded = [sem(f"kept_loaded{k}") for k in range(KEPT)]
        params_loaded = sem("params_loaded")
        eps_ready = sem("eps_ready")
        w_hi_ready = sem("w_hi_ready")
        w_lo_ready = sem("w_lo_ready")
        adj_hi_ready = sem("adj_hi_ready")
        adj_lo_by_dve = sem("adj_lo_by_dve")
        adj_lo_by_pool = sem("adj_lo_by_pool")
        piece_used = sem("piece_used")
        feat_hi_ready = sem("feat_hi_ready")
        feat_lo_ready = sem("feat_lo_ready")
        agg_hi_ready = sem("agg_hi_ready")
        agg_lo_ready = sem("agg_lo_ready")
        hid_done = [sem(f"hid_done{n}") for n in range(2)]
        hid_pre_ready = [sem(f"hid_pre_ready{n}") for n in range(2)]
        hid_ready = [sem(f"hid_ready{n}") for n in range(2)]
        hid_hi_ready = sem("hid_hi_ready")
        hid_lo_ready = sem("hid_lo_ready")
        pre_done = sem("pre_done")
        pre_ready = sem("pre_ready")
        post_ready = sem("post_ready")
        sum_ready = sem("sum_ready")
        stats_ready = sem("stats_ready")
        var_ready = sem("var_ready")
        std_ready = sem("std_ready")
        rstd_ready = sem("rstd_ready")
        normed = sem("normed")
        out_written = sem("out_written")

        def block_of(t, chunk):
            return t[:, bass.ds(chunk * CHUNK, CHUNK)]

        def by_tile(ap):
            return ap.rearrange("p (j f) -> p j f", f=P)

        def raw_piece(chunk, i):
            if i >= LOADS * LOAD:
                return adj_kept[:, bass.ds((chunk * KEPT * LOAD + (i - LOADS * LOAD)) * PIECE, PIECE)]
            return adj_raw[:, (i // LOAD) % LOAD_SLOTS, (i % LOAD) * PIECE:(i % LOAD + 1) * PIECE]

        def kept_load(chunk, k):
            return adj_kept[:, bass.ds((chunk * KEPT + k) * LOAD * PIECE, LOAD * PIECE)]

        def agg_bank(chunk, own=slice(0, TILES)):
            return agg_ps[:, bass.ds((chunk % 2) * CHUNK + own.start * P, (own.stop - own.start) * P)]

        def resid_block(chunk, own=slice(0, TILES)):
            return resid[:, bass.ds(chunk * CHUNK + own.start * P, (own.stop - own.start) * P)]

        def walk(eng, step):
            step(0, 0, 0, None, None, None)
            with eng.Fori(1, C) as c:
                step(c, c, 0, GCN, c - 1, 1)
            step(C, 0, 1, GCN, C - 1, 1)
            with eng.Fori(C, C * (PASSES - 1), 2 * C) as q0:
                with eng.Fori(1, C) as c:
                    step(q0 + c, c, 1, UV, c - 1, 0)
                step(q0 + C, 0, 0, UV, C - 1, 0)
                with eng.Fori(1, C) as c:
                    step(q0 + C + c, c, 0, VU, c - 1, 1)
                step(q0 + 2 * C, 0, 1, VU, C - 1, 1)
            with eng.Fori(1, C) as c:
                step(C * (PASSES - 1) + c, c, 1, LAST, c - 1, None)
            step(C * PASSES, None, None, LAST, C - 1, None)

        def is_first(q):
            return isinstance(q, int) and q == 0

        def in_first_pass(q, kind):
            return is_first(q) or (kind == GCN and not isinstance(q, int))

        def mlps(q):
            return q - C

        def blocks(q):
            return q + C

        def norms(q, kind):
            return q if kind == GCN else q - C * (PASSES - 2)

        def parts(chunk):
            n = LAST_PARTS if chunk is None else 1
            return [(k, slice(k * TILES // n, (k + 1) * TILES // n)) for k in range(n)]

        def cols(own):
            return slice(own.start * P, own.stop * P)

        def ps_cols(k, own):
            return slice(k * CHUNK + own.start * P, k * CHUNK + own.stop * P)

        def lo_counts(pieces, last):
            return sum(i <= last for i in pieces)

        block = ctx.enter_context(nc.Block())

        @block.sync
        def _(sp):
            def wait_split(q, last):
                by_dve = q * len(DVE_PIECES) + lo_counts(DVE_PIECES, last)
                by_pool = q * len(POOL_PIECES) + lo_counts(POOL_PIECES, last)
                if not isinstance(q, int):
                    by_dve, by_pool = sp.snap(sp.to_reg(by_dve)), sp.snap(sp.to_reg(by_pool))
                sp.wait_ge(adj_lo_by_dve, by_dve)
                if not is_first(q) or by_pool:
                    sp.wait_ge(adj_lo_by_pool, by_pool)

            def load_x(g):
                sp.dma_start(block_of(resid, g), x[g]).then_inc(x_loaded[g], 16)

            def load_params():
                for n, w in enumerate(weights):
                    sp.dma_start(w_raw[:, n, :], w).then_inc(params_loaded, 16)
                for n, b in enumerate(bias_cols):
                    sp.dma_start(b_col[:, n:n + 1], b.rearrange("(p a) -> p a", a=1)).then_inc(params_loaded, 16)
                for n, b in enumerate(bias_rows):
                    sp.dma_start(b_row[:, n, :], b.partition_broadcast(P)).then_inc(params_loaded, 16)

            def step(q, chunk, src, kind, ended, dst):
                if chunk is None:
                    sp.wait_ge(normed, norms(q, kind) - 1)
                    sp.dma_start(out[0:C - 1].rearrange("c p n -> p c n"),
                                 resid[:, 0:(C - 1) * CHUNK].rearrange("p (c n) -> p c n", c=C - 1))\
                      .then_inc(out_written, 16)
                    for k, own in parts(chunk):
                        sp.wait_ge(normed, norms(q, kind) + k)
                        sp.dma_start(out[ended][:, cols(own)], resid_block(ended, own)).then_inc(out_written, 16)
                    sp.wait_ge(out_written, 16 * (1 + LAST_PARTS))
                    return
                for g in range(LOADS):
                    if is_first(q) and g % 2 == 0:
                        load_x(g // 2)
                    if g >= LOAD_SLOTS:
                        wait_split(q, (g - LOAD_SLOTS + 1) * LOAD - 1)
                    elif not is_first(q):
                        wait_split(q - 1, (g - LOAD_SLOTS + LOADS + 1) * LOAD - 1)
                    sp.dma_start(adj_raw[:, g % LOAD_SLOTS, :], adj[chunk, g])\
                      .then_inc(adj_loaded[g % LOAD_SLOTS], 16)
                    if is_first(q) and g == LOAD_SLOTS - 1:
                        load_params()
                if is_first(q):
                    load_x(LOADS // 2)
                if in_first_pass(q, kind):
                    for k in range(KEPT):
                        sp.dma_start(kept_load(chunk, k), adj[chunk, LOADS + k]).then_inc(kept_loaded[k], 16)

            walk(sp, step)

        @block.gpsimd
        def _(pool):
            def step(q, chunk, src, kind, ended, dst):
                for i in range(PIECES + 1):
                    if is_first(q) and i % TILES == 0 and i < PIECES:
                        g = i // TILES
                        pool.wait_ge(feat_hi_ready, g + 1)
                        pool.tensor_tensor(block_of(feat_lo[0], g), block_of(resid, g),
                                           block_of(feat_hi[0], g).bitcast(F32), ALU.subtract)\
                            .then_inc(feat_lo_ready, 1)
                    if kind in (UV, VU, LAST) and i == POOL_HID:
                        for k, own in parts(chunk):
                            pool.wait_ge(hid_hi_ready, mlps(q) + k)
                            pool.tensor_tensor(in_lo[:, cols(own)], hid[:, cols(own)],
                                               in_hi[:, cols(own)].bitcast(F32), ALU.subtract)\
                                .then_inc(hid_lo_ready, 1)
                    if kind == LAST and i == POOL_SUM:
                        for k, own in parts(chunk):
                            pool.wait_ge(post_ready, mlps(q) + k)
                            pool.tensor_tensor(pre[:, cols(own)], pre[:, cols(own)], resid_block(ended, own), ALU.add)\
                                .then_inc(sum_ready, 1)
                    if kind in (GCN, UV, VU) and i == POOL_FEAT:
                        whole = block_of(resid, ended) if kind == GCN else pre[:, :]
                        pool.wait_ge(feat_hi_ready, blocks(q))
                        pool.tensor_tensor(block_of(feat_lo[dst], ended), whole,
                                           block_of(feat_hi[dst], ended).bitcast(F32), ALU.subtract)\
                            .then_inc(feat_lo_ready, 1)
                    if chunk is not None and i in POOL_PIECES:
                        pool.wait_ge(adj_hi_ready, q * PIECES + (i + 1))
                        pool.tensor_tensor(adj_lo[:, i % SPLIT_SLOTS, :], raw_piece(chunk, i),
                                           adj_hi[:, i % SPLIT_SLOTS, :].bitcast(F32), ALU.subtract)\
                            .then_inc(adj_lo_by_pool, 1)

            walk(pool, step)

        @block.scalar
        def _(act):
            def step(q, chunk, src, kind, ended, dst):
                for i in range(PIECES + 1):
                    if is_first(q) and i % TILES == 0 and i < PIECES:
                        g = i // TILES
                        act.wait_ge(x_loaded[g], 16)
                        act.activation(block_of(feat_hi[0], g), block_of(resid, g), ACT.Copy)\
                           .then_inc(feat_hi_ready, 1)
                    if is_first(q) and i == PIECES // 2:
                        act.wait_ge(params_loaded, 16 * N_PARAMS)
                        act.activation(w_hi[:, :, :], w_raw[:, 0:N_SPLIT, :], ACT.Copy).then_inc(w_hi_ready, 1)
                    if kind and i == ACT_AGG:
                        act.wait_ge(piece_used, q * PIECES)
                        to = hid if kind == GCN else in_hi
                        for k, own in parts(chunk):
                            act.activation(to[:, cols(own)], agg_bank(ended, own), ACT.Copy)\
                               .then_inc(agg_hi_ready, 1)
                    if kind in (UV, VU, LAST):
                        for n in range(2):
                            if i == ACT_HID[n]:
                                b = HID_BIAS[kind][n]
                                for k, own in parts(chunk):
                                    act.wait_ge(hid_done[n], mlps(q) + k)
                                    act.activation(hid[:, cols(own)], hid_ps[n][:, ps_cols(k, own)], ACT.Identity,
                                                   bias=b_col[:, b:b + 1]).then_inc(hid_pre_ready[n], 1)
                    if kind in (GCN, LAST) and i == ACT_STD[kind]:
                        act.wait_ge(eps_ready, 1)
                        for k, own in parts(chunk):
                            act.wait_ge(var_ready, norms(q, kind) + k)
                            act.activation(std[:, own], mean_var[:, own, 1], ACT.Sqrt, bias=eps[:, 0:1])\
                               .then_inc(std_ready, 1)
                    if chunk is None or i == PIECES:
                        continue
                    g = i // LOAD
                    if g >= LOADS and i % LOAD == 0:
                        act.wait_ge(kept_loaded[g - LOADS], 16 * (chunk + 1 if in_first_pass(q, kind) else C))
                    elif i % LOAD == 0:
                        act.wait_ge(adj_loaded[g % LOAD_SLOTS],
                                    q * (16 * LOADS // LOAD_SLOTS) + 16 * (g // LOAD_SLOTS + 1))
                    if not is_first(q) or i >= SPLIT_SLOTS:
                        act.wait_ge(piece_used, q * PIECES + (i + 1 - SPLIT_SLOTS))
                    act.activation(adj_hi[:, i % SPLIT_SLOTS, :], raw_piece(chunk, i), ACT.Copy)\
                       .then_inc(adj_hi_ready, 1)

            walk(act, step)

        @block.vector
        def _(dve):
            dve.memset(eps[:, :], EPS).then_inc(eps_ready, 1)

            def leaky_relu(t, own):
                t = t[:, cols(own)]
                return dve.scalar_tensor_tensor(t, t, SLOPE, t, ALU.mult, ALU.max)

            def statistics(q, kind, ended, k, own):
                if kind == GCN:
                    dve.wait_ge(pre_ready, q + k)
                    dve.scalar_tensor_tensor(pre[:, cols(own)], pre[:, cols(own)], 0.0, resid_block(ended, own),
                                             ALU.max, ALU.add).then_inc(sum_ready, 1)
                dve.wait_ge(sum_ready, norms(q, kind) + k)
                for j in range(own.start, own.stop):
                    last = dve.bn_stats(stats[:, j, :], pre[:, j * P:(j + 1) * P])
                last.then_inc(stats_ready, 1)

            def aggregate(q, kind, k, own):
                if isinstance(q, int):
                    dve.wait_ge(stats_ready, norms(q, kind) + k)
                for j in range(own.start, own.stop):
                    last = dve.bn_aggr(mean_var[:, j, :], stats[:, j, :])
                last.then_inc(var_ready, 1)

            def normalise(q, kind, ended, k, own):
                dve.wait_ge(std_ready, norms(q, kind) + k)
                dve.reciprocal(rstd[:, own], std[:, own]).then_inc(rstd_ready, 1)
                dve.wait_ge(rstd_ready, norms(q, kind) + k)
                for j in range(own.start, own.stop):
                    last = dve.tensor_scalar(resid_block(ended, slice(j, j + 1)), pre[:, j * P:(j + 1) * P],
                                             mean_var[:, j, 0:1], rstd[:, j:j + 1], ALU.subtract, ALU.mult)
                last.then_inc(normed, 1)

            def step(q, chunk, src, kind, ended, dst):
                for i in range(PIECES + 1):
                    if is_first(q) and i == PIECES // 2:
                        dve.wait_ge(w_hi_ready, 1)
                        dve.tensor_tensor(w_lo[:, :, :], w_raw[:, 0:N_SPLIT, :], w_hi[:, :, :].bitcast(F32), ALU.subtract)\
                           .then_inc(w_lo_ready, 1)
                    if kind in (UV, VU, LAST) and i == DVE_AGG:
                        for k, own in parts(chunk):
                            dve.wait_ge(agg_hi_ready, q + len(parts(chunk)) - 1)
                            dve.tensor_tensor(in_lo[:, cols(own)], agg_bank(ended, own),
                                              in_hi[:, cols(own)].bitcast(F32), ALU.subtract)\
                               .then_inc(agg_lo_ready, 1)
                    if kind in (UV, VU, LAST):
                        for n in range(2):
                            if i == DVE_HID[n]:
                                for k, own in parts(chunk):
                                    dve.wait_ge(hid_pre_ready[n], mlps(q) + k)
                                    leaky_relu(hid, own).then_inc(hid_ready[n], 1)
                                    if n == 0:
                                        dve.wait_ge(hid_ready[0], mlps(q) + k)
                                        dve.tensor_copy(in_hi[:, cols(own)], hid[:, cols(own)])\
                                           .then_inc(hid_hi_ready, 1)
                    if kind and i == DVE_PRE[kind]:
                        b = PRE_BIAS[kind]
                        for k, own in parts(chunk):
                            n_own = own.stop - own.start
                            dve.wait_ge(pre_done, q + k)
                            dve.tensor_tensor(by_tile(pre[:, cols(own)]), by_tile(pre_ps[:, ps_cols(k, own)]),
                                              b_row[:, b:b + 1, :].to_broadcast([P, n_own, P]), ALU.add)\
                               .then_inc(pre_ready, 1)
                    if kind in (GCN, LAST) and i == DVE_STATS[kind]:
                        for k, own in parts(chunk):
                            statistics(q, kind, ended, k, own)
                    if kind in (GCN, LAST) and i == DVE_STATS[kind] + 1:
                        for k, own in parts(chunk):
                            aggregate(q, kind, k, own)
                    if kind in (GCN, LAST) and i == DVE_NORM[kind]:
                        for k, own in parts(chunk):
                            normalise(q, kind, ended, k, own)
                    if kind == GCN and i == DVE_NORM[kind]:
                        dve.wait_ge(normed, norms(q, kind))
                        dve.tensor_copy(block_of(feat_hi[dst], ended), block_of(resid, ended))\
                           .then_inc(feat_hi_ready, 1)
                    if kind in (UV, VU, LAST) and i == DVE_LEAKY:
                        for k, own in parts(chunk):
                            dve.wait_ge(pre_ready, q + k)
                            leaky_relu(pre, own).then_inc(post_ready, 1)
                    if kind in (UV, VU) and i == DVE_FEAT:
                        dve.wait_ge(post_ready, mlps(q))
                        dve.tensor_copy(block_of(feat_hi[dst], ended), pre[:, :]).then_inc(feat_hi_ready, 1)
                    if chunk is not None and i in DVE_PIECES:
                        if kind in (GCN, LAST) and i == DVE_STATS[kind]:
                            dve.wait_ge(stats_ready, norms(q, kind))
                        dve.wait_ge(adj_hi_ready, q * PIECES + (i + 1))
                        dve.tensor_tensor(adj_lo[:, i % SPLIT_SLOTS, :], raw_piece(chunk, i),
                                          adj_hi[:, i % SPLIT_SLOTS, :].bitcast(F32), ALU.subtract)\
                           .then_inc(adj_lo_by_dve, 1)

            walk(dve, step)

        @block.tensor
        def _(pe):
            def product(to, left, right, start=True, stop=True):
                (l_hi, l_lo), (r_hi, r_lo) = left, right
                pe.matmul(to, l_hi, r_hi, start=start, stop=False)
                pe.matmul(to, l_hi, r_lo, start=False, stop=False)
                return pe.matmul(to, l_lo, r_hi, start=False, stop=stop)

            def hidden(n, w, k, own):
                product(hid_ps[n][:, ps_cols(k, own)], (w_hi[:, w, :], w_lo[:, w, :]), (in_hi[:, cols(own)], in_lo[:, cols(own)]))\
                    .then_inc(hid_done[n], 1)

            def last_layer(w, k, own):
                for j in range(own.start, own.stop):
                    last = pe.matmul(pre_ps[:, ps_cols(k, slice(j, j + 1))], hid[:, j * P:(j + 1) * P], w_raw[:, w, :],
                                     start=True, stop=True)
                last.then_inc(pre_done, 1)

            def step(q, chunk, src, kind, ended, dst):
                bank = agg_bank(chunk) if chunk is not None else None
                for i in range(PIECES + 1):
                    if is_first(q) and i == PIECES - 1:
                        pe.wait_ge(w_lo_ready, 1)
                    for k, own in parts(chunk):
                        if kind == GCN and i == PE_GCN:
                            pe.wait_ge(agg_hi_ready, q)
                            last_layer(LAYERS[kind][0], k, own)
                        if kind in (UV, VU, LAST):
                            if i == PE_LAYER[0]:
                                pe.wait_ge(agg_lo_ready, mlps(q) + k)
                                hidden(0, LAYERS[kind][0], k, own)
                            if i == PE_LAYER[1]:
                                pe.wait_ge(hid_lo_ready, mlps(q) + k)
                                hidden(1, LAYERS[kind][1], k, own)
                            if i == PE_LAYER[2]:
                                pe.wait_ge(hid_ready[1], mlps(q) + k)
                                last_layer(LAYERS[kind][2], k, own)
                    if chunk is None or i == PIECES:
                        continue
                    if isinstance(chunk, int) and i % TILES == 0:
                        pe.wait_ge(feat_hi_ready, q + (i // TILES + 1))
                        pe.wait_ge(feat_lo_ready, q + (i // TILES + 1))
                    pieces, ready = ((POOL_PIECES, adj_lo_by_pool) if i in POOL_PIECES
                                     else (DVE_PIECES, adj_lo_by_dve))
                    pe.wait_ge(ready, q * len(pieces) + lo_counts(pieces, i))
                    tile, slot = slice(i * P, (i + 1) * P), i % SPLIT_SLOTS
                    last = product(bank, (feat_hi[src][:, tile], feat_lo[src][:, tile]),
                                   (adj_hi[:, slot, :], adj_lo[:, slot, :]), start=i == 0, stop=i == PIECES - 1)
                    last.then_inc(piece_used, 1)

            walk(pe, step)


def kernel(x, adj, L0_gnn_kernel, L0_gnn_bias, **mlps):
    import numpy as _np
    import concourse.bacc as _bacc
    from concourse.bass_utils import run_bass_kernel_spmd as _run

    nodes, features = x.shape
    chunks = nodes // CHUNK
    node = (chunks, P, TILES)
    arrays = {"x": _np.ascontiguousarray(x).reshape(chunks, P, TILES * features)}
    to_from = _np.asarray(adj).reshape(node + (chunks, P, TILES // LOAD, LOAD))
    arrays["adj"] = _np.ascontiguousarray(to_from.transpose(0, 3, 5, 4, 6, 2, 1))\
        .reshape(chunks, chunks * TILES // LOAD, P, LOAD * PIECE)
    arrays["gcn_w"] = _np.ascontiguousarray(L0_gnn_kernel)
    arrays["gcn_b"] = _np.ascontiguousarray(L0_gnn_bias)
    for tag in ("uv", "vu"):
        for part in ("W1", "b1", "W2", "b2", "W3", "b3"):
            arrays[f"{tag}_{part}"] = _np.ascontiguousarray(mlps[f"L1_gnn_{tag}_{part}"])

    nc = _bacc.Bacc("TRN2", target_bir_lowering=False, num_devices=1, dynamic_dma_scratch_size=1024)
    aps = {name: nc.dram_tensor(f"in_{name}", a.shape, mybir.dt.from_np(a.dtype), kind="ExternalInput").ap()
           for name, a in arrays.items()}
    out = nc.dram_tensor("out", arrays["x"].shape, F32, kind="ExternalOutput").ap()
    uv, vu = ({part: aps[f"{tag}_{part}"] for part in ("W1", "b1", "W2", "b2", "W3", "b3")} for tag in ("uv", "vu"))
    gnn_kernel(nc, aps["x"], aps["adj"], aps["gcn_w"], aps["gcn_b"], uv, vu, out)
    ran = _run(nc, [{f"in_{name}": a for name, a in arrays.items()}], core_ids=[0])
    return ran.results[0]["out"].reshape(nodes, features)
```
